# Optimizing a Trainium2 kernel written in Bass

```python
import numpy as np
import jax
import jax.numpy as jnp

def _softmax(x, axis=-1):
    return jax.nn.softmax(x, axis=axis)

def _gelu(x):
    return jax.nn.gelu(x, approximate=True)

def _silu(x):
    return jax.nn.silu(x)

def _sigmoid(x):
    return jax.nn.sigmoid(x)

def _layernorm(x, axis=-1, eps=1e-05):
    m = jnp.mean(x, axis=axis, keepdims=True)
    v = jnp.var(x, axis=axis, keepdims=True)
    return (x - m) / jnp.sqrt(v + eps)

def _scatter_add(tgt, idx, src, axis=0):
    return tgt.at[idx].add(src)

def _segment_sum(src, seg, n):
    return jax.ops.segment_sum(src, seg, n)
kernel_name = 'mk_gnn_ffn_d1_gnn_r8_80a356'

def setup_inputs(seed: int=0):
    np.random.seed(seed)
    _w = jnp.asarray

    def _rec_inputs():
        import jax
        import jax.numpy as jnp
        _gk = jax.random.key(seed)
        x = -0.0003713 + 1 * jax.random.normal(jax.random.fold_in(_gk, 1), (6250, 256), jnp.float32)
        src = jax.random.randint(jax.random.fold_in(_gk, 2), (200000,), 0, 6250, jnp.int32)
        dst = jnp.minimum((6250 * jax.random.uniform(jax.random.fold_in(_gk, 3), (200000,)) ** 2.0).astype(jnp.int32), 49999)
        _o = jnp.argsort(dst, stable=True)
        src = src[_o]
        dst = dst[_o]
        return (x, src, dst)
    x, src, dst = _rec_inputs()

    def _L0_gnn_setup():
        import jax, jax.numpy as jnp
        import numpy as np
        N_NODES = 6250
        N_EDGES = 100000
        D_MODEL = 256
        H = 8
        D_K = 32
        key = jax.random.key(seed)
        kx, kq, kk, kv, ks, kd = jax.random.split(key, 6)
        scale = 1.0 / np.sqrt(D_MODEL)
        x = jax.random.normal(kx, (N_NODES, D_MODEL), dtype=jnp.float32)
        Wq = jax.random.normal(kq, (D_MODEL, H * D_K), dtype=jnp.float32) * scale
        Wk = jax.random.normal(kk, (D_MODEL, H * D_K), dtype=jnp.float32) * scale
        Wv = jax.random.normal(kv, (D_MODEL, H * D_K), dtype=jnp.float32) * scale
        src = jax.random.randint(ks, (N_EDGES,), 0, N_NODES, dtype=jnp.int32)
        dst = jax.random.randint(kd, (N_EDGES,), 0, N_NODES, dtype=jnp.int32)
        return {'x': x, 'Wq': Wq, 'Wk': Wk, 'Wv': Wv, 'src': src, 'dst': dst}
    _L0_gnn_all = _L0_gnn_setup()
    _L0_gnn_in = {k: v for k, v in _L0_gnn_all.items() if k in ('Wq', 'Wk', 'Wv')}
    del _L0_gnn_all

    def _L0_ffn_setup():
        import jax, jax.numpy as jnp
        import numpy as np
        E, D, H, TOP_K = (6, 256, 256, 2)
        ROUTER_H = D // 2
        key = jax.random.key(seed)
        ks = jax.random.split(key, 12)
        s = 1.0 / np.sqrt(D)
        sh = 1.0 / np.sqrt(H)
        sr = 1.0 / np.sqrt(ROUTER_H)
        return {'features': jax.random.normal(ks[0], (8, 512, D), dtype=jnp.float32), 'router_w1': jax.random.uniform(ks[1], (D, ROUTER_H), jnp.float32, -s, s), 'router_b1': jnp.zeros((ROUTER_H,), jnp.float32), 'router_w2': jax.random.uniform(ks[2], (ROUTER_H, E), jnp.float32, -sr, sr), 'router_b2': jnp.zeros((E,), jnp.float32), 'expert_w1': jax.random.uniform(ks[3], (E, D, H), jnp.float32, -s, s), 'expert_b1': jnp.zeros((E, H), jnp.float32), 'expert_w2': jax.random.uniform(ks[4], (E, H, H), jnp.float32, -sh, sh), 'expert_b2': jnp.zeros((E, H), jnp.float32), 'expert_w3': jax.random.uniform(ks[5], (E, H, D), jnp.float32, -sh, sh), 'expert_b3': jnp.zeros((E, D), jnp.float32)}
    _L0_ffn_all = _L0_ffn_setup()
    _L0_ffn_in = {k: v for k, v in _L0_ffn_all.items() if k in ('router_w1', 'router_b1', 'router_w2', 'router_b2', 'expert_w1', 'expert_b1', 'expert_w2', 'expert_b2', 'expert_w3', 'expert_b3')}
    del _L0_ffn_all
    return {'x': x, 'src': src, 'dst': dst, 'L0_gnn_Wq': _L0_gnn_in['Wq'], 'L0_gnn_Wk': _L0_gnn_in['Wk'], 'L0_gnn_Wv': _L0_gnn_in['Wv'], 'L0_ffn_router_w1': _L0_ffn_in['router_w1'], 'L0_ffn_router_b1': _L0_ffn_in['router_b1'], 'L0_ffn_router_w2': _L0_ffn_in['router_w2'], 'L0_ffn_router_b2': _L0_ffn_in['router_b2'], 'L0_ffn_expert_w1': _L0_ffn_in['expert_w1'], 'L0_ffn_expert_b1': _L0_ffn_in['expert_b1'], 'L0_ffn_expert_w2': _L0_ffn_in['expert_w2'], 'L0_ffn_expert_b2': _L0_ffn_in['expert_b2'], 'L0_ffn_expert_w3': _L0_ffn_in['expert_w3'], 'L0_ffn_expert_b3': _L0_ffn_in['expert_b3']}

def reference(x, src, dst, L0_gnn_Wq, L0_gnn_Wk, L0_gnn_Wv, L0_ffn_router_w1, L0_ffn_router_b1, L0_ffn_router_w2, L0_ffn_router_b2, L0_ffn_expert_w1, L0_ffn_expert_b1, L0_ffn_expert_w2, L0_ffn_expert_b2, L0_ffn_expert_w3, L0_ffn_expert_b3):
    import jax
    import jax.numpy as jnp

    def _L0_gnn_ref(x, Wq, Wk, Wv, src, dst):
        import jax, jax.numpy as jnp
        import numpy as np
        N_NODES = 6250
        N_EDGES = 100000
        D_MODEL = 256
        H = 8
        D_K = 32
        q = (x @ Wq).reshape(N_NODES, H, D_K)
        k = (x @ Wk).reshape(N_NODES, H, D_K)
        v = (x @ Wv).reshape(N_NODES, H, D_K)
        score = jnp.sum(k[src] * q[dst], axis=-1, keepdims=True)
        score = jnp.exp(jnp.clip(score / np.sqrt(D_K), -5.0, 5.0))
        wv = jax.ops.segment_sum(v[src] * score, dst, num_segments=N_NODES)
        z = jax.ops.segment_sum(score, dst, num_segments=N_NODES)
        out = wv / (z + 1e-09)
        return out.reshape(N_NODES, H * D_K)

    def _L0_ffn_ref(features, router_w1, router_b1, router_w2, router_b2, expert_w1, expert_b1, expert_w2, expert_b2, expert_w3, expert_b3):
        import jax, jax.numpy as jnp
        import numpy as np
        E, D, H, TOP_K = (6, 256, 256, 2)
        ROUTER_H = D // 2
        rh = jax.nn.relu(features @ router_w1 + router_b1)
        expert_logits = jax.nn.softmax(rh @ router_w2 + router_b2, axis=-1)
        top_w, top_i = jax.lax.top_k(expert_logits, TOP_K)
        routing_weights = jax.nn.softmax(top_w, axis=-1)
        h1 = jax.nn.relu(jnp.einsum('bsd,edh->bseh', features, expert_w1) + expert_b1)
        h2 = jax.nn.relu(jnp.einsum('bseh,ehf->bsef', h1, expert_w2) + expert_b2)
        expert_out = jnp.einsum('bsef,efo->bseo', h2, expert_w3) + expert_b3
        sel = jnp.take_along_axis(expert_out, top_i[:, :, :, None], axis=2)
        combined = jnp.sum(sel * routing_weights[..., None], axis=2)
        return combined
    x = x + _L0_gnn_ref(_layernorm(x, axis=-1), L0_gnn_Wq, L0_gnn_Wk, L0_gnn_Wv, src, dst)
    x = x + _L0_ffn_ref(_layernorm(x, axis=-1)[None], L0_ffn_router_w1, L0_ffn_router_b1, L0_ffn_router_w2, L0_ffn_router_b2, L0_ffn_expert_w1, L0_ffn_expert_b1, L0_ffn_expert_w2, L0_ffn_expert_b2, L0_ffn_expert_w3, L0_ffn_expert_b3)[0]
    return x

_drawn_inputs = setup_inputs


def setup_inputs(seed=0):
    import zlib

    import numpy as np

    out = dict(_drawn_inputs(seed))
    spreads = {'L0_ffn_router_b1': (0.0, 0.1),
     'L0_ffn_router_b2': (0.0, 0.1),
     'L0_ffn_expert_b1': (0.0, 0.711),
     'L0_ffn_expert_b2': (0.0, 0.301),
     'L0_ffn_expert_b3': (0.0, 0.1)}
    factors = {}
    for name, (base, spread) in spreads.items():
        noise = np.random.default_rng([zlib.crc32(name.encode()), seed]).standard_normal(out[name].shape)
        drawn = base * np.exp(spread * noise) if base else spread * noise
        out[name] = jnp.asarray(drawn.astype(out[name].dtype))
    for name, factor in factors.items():
        out[name] = (out[name] * factor).astype(out[name].dtype)
    return out
```

```python
from contextlib import ExitStack

import concourse.bass as bass
from concourse import mybir

ALU = mybir.AluOpType
ACT = mybir.ActivationFunctionType
F32 = mybir.dt.float32
F32R = mybir.dt.float32r
BF16 = mybir.dt.bfloat16
I32 = mybir.dt.int32
I16 = mybir.dt.int16
AX = mybir.AxisListType.X
RMAX = bass.bass_isa.ReduceOp.max

P = 128
N, D, H, DK = 6250, 256, 8, 32
E = 200000
NB = -(-N // P)
NT = NB + 1
HB = -(-NB // 2)
UNIT = 32
UPP = -(-E // (UNIT * P))
UPAD = UPP * P
TPH = 2
HALF = TPH * P
STEP = 2 * HALF
UPS = STEP // UNIT
EPAD = UPAD * UNIT + 3 * STEP
MAXC = UPAD // UPS + 2
FAR = 1 << 14
KV = 2 * D
WZ = D + H
XC = 5
TPX = NT // XC
NE, RH = 6, 128
GB = 7
NG = NB // GB
GT = GB * P
HT = GT // 2
USES = 2 + 8 * NE
PAIRS = -(-GB // 2)
SUMS = (NE + 1) * PAIRS
GATES, EX_AT, EE_AT = 23, 3, 17
PREP = 4 + 2 * GB + 3
EPS = 1e-5
CLIP = 5.0 * DK ** 0.5
FIRST, COUNT, BEFORE, LOADS = range(4)


def counter():
    n = [0]

    def reaches(more=1):
        n[0] += more
        return n[0]
    return reaches


def gnn_ffn(nc, x, edges, wkvq, rw1, rw2, rb2, w1, w2, w3, eb3, cols, ident_in, lower_in, kv_table, out):
    with ExitStack() as ctx:
        def sb(name, shape, dt=F32):
            return ctx.enter_context(nc.sbuf_tensor(name, shape, dt))

        def sem(name):
            return ctx.enter_context(nc.semaphore(name))

        x_sb = sb("x_sb", [P, NT, D])
        q_sb = sb("q_sb", [P, NT, D])
        z_sb = sb("z_sb", [P, NB, H])
        idx = sb("idx", [P, 4, TPH, 2], I32)
        oh = sb("oh", [P, 2, TPH, P], BF16)
        oh_t = sb("oh_t", [P, 2, TPH, P], F32R)
        qhl = sb("qhl", [P, 3, 2, D], F32R)
        score = sb("score", [P, 2, TPH, H])
        clipped = sb("clipped", [P, 2, TPH, H])
        zero = sb("zero", [P, WZ])
        ident = sb("ident", [P, P])
        identb = sb("identb", [P, P], BF16)
        table = sb("table", [P, 4, NB], I32)
        odd = sb("odd", [P, 1], I32)
        pairs = sb("pairs", [P, 1], I32)
        w2_sb = sb("w2_sb", [P, NE, 2, D])
        w3_sb = sb("w3_sb", [P, NE, 2, D])
        rw1_sb = sb("rw1_sb", [P, 2, RH])
        rw2_sb = sb("rw2_sb", [P, NE])
        rb2_sb = sb("rb2_sb", [P, NE])
        eb3_sb = sb("eb3_sb", [NE, D])
        cols_sb = sb("cols_sb", [P, 4 * NE + 1])
        lower = sb("lower", [P, NE, NE])
        bn = sb("bn", [P, NT, 6])
        mv = sb("mv", [P, NT, 2])
        ve = sb("ve", [P, NT])
        sd = sb("sd", [P, NT])
        rstd = sb("rstd", [P, NT])
        def parts(name, size):
            whole = sb(name, [P, size])
            used = [0]

            def part(*shape):
                if shape == (0,):
                    used[0] = 0
                    return None
                n = 1
                for k in shape:
                    n *= k
                at = used[0]
                used[0] += n
                assert used[0] <= size, (name, used[0])
                v = whole[:, at:at + n]
                if len(shape) > 1:
                    names = " ".join("abcd"[:len(shape)])
                    v = v.rearrange(f"p ({names}) -> p {names}", **dict(zip("abcd", shape)))
                return v
            return part

        part = parts("stage_b_or_c", 4 * TPH * KV + NT * P // 2 + 6 * D + 2 * TPH * (WZ + P) + TPH * D)
        ring = part(4, TPH, KV)
        nodes = part(NT * P // 2).bitcast(I16)
        wkvq_sb = part(2, 3 * D)
        oh_sum = part(2, TPH, P)
        wv = part(2, TPH, WZ)
        prod = part(TPH, D)
        part(0)
        ft = part(2, 2, GT)
        xn3 = part(GB, D)
        h1, h2 = part(2, GT), part(2, GT)
        rh = part(GT)
        lg, ex, pr, sel1, sel2, gate, rank, tmp = (part(GB, NE) for _ in range(8))
        above, equal = (part(GB, NE, NE) for _ in range(2))
        m0, se, rse, t1, t2, dd, ee, e1, wt1, wt2 = (part(GB) for _ in range(10))
        ze, zr = (part(GB, H) for _ in range(2))

        part = parts("stage_a_or_c", 2 * (2 * D + KV) + 3 * UPP + 12 * NB + 2 * HB * UPP)
        xn = part(2, D)
        xt = part(2, 2, P)
        kvs = part(2, KV)
        umin, umax, unit_f = (part(UPP) for _ in range(3))
        lo_f, hi_f = part(NB), part(NB)
        inter, inter2 = part(HB, UPP), part(HB, UPP)
        ends, ends_all = part(2, NB), part(2, NB)
        tf = part(6, NB)
        part(0)
        w1_sb = part(NE, 2, D)
        gt = part(GT)
        edges_sb = ring.rearrange("p a b c -> p (a b c)").bitcast(I32)[:, 0:UPP * UNIT * 2].rearrange(
            "p (u e c) -> p u e c", e=UNIT, c=2)
        iota_i = sb("iota_i", [P, 2 * NB + UPP], I32)

        bank = [ctx.enter_context(nc.psum_tensor(f"bank{i}", [P, 512], F32)) for i in range(6)]
        acc = ctx.enter_context(nc.psum_tensor("acc", [P, 2, 512], F32))

        x_in = [sem(f"x_in{c}") for c in range(XC)]
        w_in = sem("w_in")
        e_in = sem("e_in")
        c_in = sem("c_in")
        f_in = sem("f_in")
        iota_done = sem("iota_done")
        bounds = sem("bounds_steps")
        ends_ready = sem("ends_ready")
        ends_reduced = sem("ends_reduced")
        table_ready = sem("table_ready")
        stats = sem("stats_steps")
        ve_ready = sem("ve_ready")
        sd_ready = sem("sd_ready")
        rstd_ready = sem("rstd_ready")
        xn_done = [sem(f"xn_done{u}") for u in range(2)]
        tp_done = [sem(f"tp_done{u}") for u in range(2)]
        xt_done = [sem(f"xt_done{u}") for u in range(2)]
        kvp_done = [sem(f"kvp_done{u}") for u in range(2)]
        qp_done = [sem(f"qp_done{u}") for u in range(2)]
        kvs_done = [sem(f"kvs_done{u}") for u in range(2)]
        kv_out = [sem(f"kv_out{u}") for u in range(2)]
        q_kept = [sem(f"q_kept{u}") for u in range(2)]
        idx_in = [sem(f"idx_in{s}") for s in range(4)]
        kv_in = [sem(f"kv_in{s}") for s in range(4)]
        idx_seen = sem("idx_seen")
        kv_seen = sem("kv_seen")
        oh_done = [sem(f"oh_done{h}") for h in range(2)]
        ot_done = [sem(f"ot_done{h}") for h in range(2)]
        oht_done = [sem(f"oht_done{h}") for h in range(2)]
        keep_done = [sem(f"keep_done{h}") for h in range(2)]
        spread_done = [sem(f"spread_done{h}") for h in range(2)]
        prod_done = [sem(f"prod_done{h}") for h in range(2)]
        score_done = [sem(f"score_done{h}") for h in range(2)]
        clip_done = [sem(f"clip_done{h}") for h in range(2)]
        weight_done = [sem(f"weight_done{h}") for h in range(2)]
        wv_done = [sem(f"wv_done{h}") for h in range(2)]
        sum_done = [sem(f"sum_done{h}") for h in range(2)]
        acc_done = sem("acc_done")
        flushed = sem("flushed")
        qhi_done = sem("qhi_done")
        qlo_done = sem("qlo_done")
        zero_done = sem("zero_done")
        edges_done = sem("edges_done")
        f_prep = sem("f_prep")
        f_sqrt = sem("f_sqrt")
        f_turned = sem("f_turned")
        f_ft = sem("f_ft")
        f_col = sem("f_col")
        f_relu = sem("f_relu")
        f_logits = sem("f_logits")
        f_gate = sem("f_gate")
        f_exp = sem("f_exp")
        f_gturned = sem("f_gturned")
        f_gt = sem("f_gt")
        f_last = sem("f_last")
        f_sum = sem("f_sum")
        f_out = sem("f_out")
        f_mark = sem("f_mark")
        sp_mark = sem("sp_mark")

        def inside(value, most):
            return nc.s_assert_within(value, 0, most, skip_runtime_bounds_check_because="it follows from the table of stretches")

        def ds(at, n=1):
            return bass.ds(at, n)

        block = ctx.enter_context(nc.Block())

        @block.sync
        def _(sp):
            sp.dma_start(edges_sb, edges[0:UPAD * UNIT, :].rearrange("(p u e) c -> p u e c", p=P, e=UNIT)).then_inc(e_in, 16)
            for c in range(XC):
                sp.dma_start(x_sb[:, c * TPX:(c + 1) * TPX, :],
                             x[c * TPX * P:(c + 1) * TPX * P, :].rearrange("(t p) d -> p t d", p=P)).then_inc(x_in[c], 16)
                if c == 0:
                    sp.dma_start(ident[:, :], ident_in).then_inc(c_in, 16)
                    sp.dma_start(wkvq_sb[:, :, :], wkvq.rearrange("(c p) n -> p c n", p=P)).then_inc(w_in, 16)
            for to, of in ((w2_sb, w2), (w3_sb, w3)):
                sp.dma_start(to[:, :, :, :], of.rearrange("e (c p) n -> p e c n", p=P)).then_inc(f_in, 16)
            sp.dma_start(rw1_sb[:, :, :], rw1.rearrange("(c p) n -> p c n", p=P)).then_inc(f_in, 16)
            sp.dma_start(rw2_sb[:, :], rw2).then_inc(f_in, 16)
            sp.dma_start(rb2_sb[:, :], rb2.rearrange("(a n) -> a n", a=1).to_broadcast([P, NE])).then_inc(f_in, 16)
            sp.dma_start(eb3_sb[:, :], eb3).then_inc(f_in, 16)
            sp.dma_start(cols_sb[:, :], cols).then_inc(f_in, 16)
            sp.dma_start(lower[:, :, :].rearrange("p a b -> p (a b)"), lower_in.to_broadcast([P, NE * NE])).then_inc(f_in, 16)

            def store(i):
                for u in range(2):
                    sp.wait_ge(kvs_done[u], i + 2)
                    sp.dma_start(kv_table[ds((2 * i + u) * P, P), :], kvs[:, u, :]).then_inc(kv_out[u], 16)
            with sp.Fori(0, NT // 2) as i:
                store(i)

            for u in range(2):
                sp.wait_ge(q_kept[u], NT // 2 + 1)
                sp.wait_ge(kv_out[u], 16 * (NT // 2))
            sp.wait_ge(table_ready, 1)
            sp.dma_start(w1_sb, w1.rearrange("e (c p) n -> p e c n", p=P)).then_inc(f_in, 16)

            with sp.Fori(0, NB) as b:
                first = sp.value_load(table[0:1, FIRST, ds(b)], min_val=0, max_val=UPAD - 1)
                loads = sp.value_load(table[0:1, LOADS, ds(b)], min_val=1, max_val=MAXC)
                before = sp.value_load(table[0:1, BEFORE, ds(b)], min_val=0, max_val=NB * (MAXC))
                with sp.Fori(0, loads) as j:
                    g = sp.snap(before + j)
                    start = inside(sp.snap(first * UNIT + j * STEP), EPAD - STEP)

                    starts = [start, sp.snap(start + HALF)]
                    landed = [sp.snap(2 * g + 1), sp.snap(2 * g + 2)]
                    read = sp.snap(g + 1)

                    def load(slots):
                        for h in range(2):
                            sp.wait_ge(kv_seen, landed[h])
                            sp.sem_inc(sp_mark, 1)
                            sp.wait_ge(oh_done[h], read)
                            sp.dma_start(idx[:, slots + h, :, :].rearrange("p t c -> p (t c)"),
                                         edges[ds(starts[h], HALF), :].rearrange("(p t) c -> p (t c)", t=TPH)
                                         ).then_inc(idx_in[slots + h], 16)
                    with sp.If((g % 2) == 0):
                        load(0)
                    with sp.Else():
                        load(2)

            with sp.Fori(0, NG) as G:
                sp.wait_ge(f_sum, (G + 1) * SUMS + 2)
                sp.dma_start(out[ds(G * GT, GT), :].rearrange("(t p) d -> p t d", p=P),
                             x_sb[:, ds(G * GB, GB), :]).then_inc(f_out, 16)
            sp.wait_ge(f_out, 16 * NG)

        @block.gpsimd
        def _(pool):
            nc.gpsimd.iota(nodes[:, :], pattern=[[1, NT * P]], base=0, channel_multiplier=0).then_inc(iota_done, 1)
            nc.gpsimd.iota(iota_i[:, 0:NB], pattern=[[P, NB]], base=0, channel_multiplier=0).then_inc(iota_done, 1)
            nc.gpsimd.iota(iota_i[:, NB:2 * NB], pattern=[[P, NB]], base=P - 1, channel_multiplier=0).then_inc(iota_done, 1)
            nc.gpsimd.iota(iota_i[:, 2 * NB:], pattern=[[1, UPP]], base=0, channel_multiplier=UPP).then_inc(iota_done, 1)

            pool.wait_ge(ends_ready, 1)
            nc.gpsimd.partition_all_reduce(ends_all, ends, P, RMAX).then_inc(ends_reduced, 1)

            def gather(s, i, g):
                pool.wait_ge(idx_in[s], 16 * (i + 1))
                pool.wait_ge(wv_done[s % 2], g + 1)
                pool.sem_inc(idx_seen, 1)
                for t in range(TPH):
                    nc.gpsimd.indirect_dma_start(ring[:, s, t, :], None, kv_table,
                                                 bass.IndirectOffsetOnAxis(idx[:, s, t, 0:1], 0)).then_inc(kv_in[s], 16)

            def landed(s, i):
                pool.wait_ge(kv_in[s], 16 * TPH * (i + 1))
                pool.sem_inc(kv_seen, 1)

            pool.sem_inc(kv_seen, 4)
            for u in range(2):
                pool.wait_ge(kv_out[u], 16 * (NT // 2))
            pool.wait_ge(table_ready, 1)
            n = pool.value_load(pairs[0:1, 0:1], min_val=1, max_val=NB * (MAXC) // 2)
            gather(0, 0, 0)
            gather(1, 0, 0)
            with pool.Fori(0, n) as i:
                landed(0, i)
                gather(2, i, 2 * i + 1)
                landed(1, i)
                gather(3, i, 2 * i + 1)
                landed(2, i)
                gather(0, i + 1, 2 * i + 2)
                landed(3, i)
                gather(1, i + 1, 2 * i + 2)
            for s in range(2):
                pool.wait_ge(kv_in[s], 16 * TPH * (n + 1))
            pool.sem_inc(edges_done, 1)

        @block.tensor
        def _(pe):
            pe.wait_ge(c_in, 16)
            pe.wait_ge(w_in, 16)
            for u in range(2):
                pe.sem_inc(tp_done[u], 1)

            def turn(i, u):
                pe.wait_ge(xn_done[u], i + 1)
                pe.wait_ge(xt_done[u], i + 1)
                for c in range(2):
                    ins = nc.tensor.transpose(bank[u][:, c * P:(c + 1) * P], xn[:, u, c * P:(c + 1) * P], ident[:, :])
                ins.then_inc(tp_done[u], 1)

            def project(i, u):
                pe.wait_ge(xt_done[u], i + 2)
                pe.wait_ge(kvs_done[u], i + 1)
                for c in range(2):
                    ins = nc.tensor.matmul(bank[2 + u][:, :], xt[:, u, c, :], wkvq_sb[:, c, 0:KV], start=c == 0, stop=c == 1)
                ins.then_inc(kvp_done[u], 1)
                pe.wait_ge(q_kept[u], i + 1)
                for c in range(2):
                    ins = nc.tensor.matmul(bank[4 + u][:, 0:D], xt[:, u, c, :], wkvq_sb[:, c, KV:], start=c == 0, stop=c == 1)
                ins.then_inc(qp_done[u], 1)

            turn(0, 0)
            with pe.Fori(0, NT // 2 - 1) as i:
                turn(i, 1)
                project(i, 0)
                turn(i + 1, 0)
                project(i, 1)
            turn(NT // 2 - 1, 1)
            project(NT // 2 - 1, 0)
            project(NT // 2 - 1, 1)

            pe.wait_ge(zero_done, 2)
            for h in range(2):
                pe.sem_inc(sum_done[h], 1)

            def turn_onehot(g, h):
                pe.wait_ge(oh_done[h], g + 3)
                pe.wait_ge(oht_done[h], g + 1)
                for t in range(TPH):
                    ins = nc.tensor.transpose(bank[h][:, :].bitcast(BF16)[:, t * P:(t + 1) * P], oh[:, h, t, :], identb[:, :])
                ins.then_inc(ot_done[h], 1)

            def spread(g, h, qs):
                pe.wait_ge(oht_done[h], g + 2)
                pe.wait_ge(prod_done[h], g + 1)
                for t in range(TPH):
                    for piece in range(2):
                        ins = nc.tensor.matmul(bank[2 + h][:, t * D:(t + 1) * D], oh_t[:, h, t, :],
                                               qhl[:, ds(qs), piece, :].rearrange("p a d -> p (a d)"),
                                               start=piece == 0, stop=piece == 1)
                ins.then_inc(spread_done[h], 1)

            def add_up(g, h, sums):
                pe.wait_ge(wv_done[h], g + 3)
                pe.wait_ge(keep_done[h], g + 1)
                for t in range(TPH):
                    ins = nc.tensor.matmul(sums, oh_sum[:, h, t, :], wv[:, h, t, :], start=False, stop=False,
                                           skip_group_check=True)
                ins.then_inc(sum_done[h], 1)

            pe.wait_ge(table_ready, 1)
            pe.wait_ge(qlo_done, 1)
            for h in range(2):
                turn_onehot(0, h)
                spread(0, h, 0)
            with pe.Fori(0, NB) as b:
                count = pe.value_load(table[0:1, COUNT, ds(b)], min_val=1, max_val=MAXC)
                before = pe.value_load(table[0:1, BEFORE, ds(b)], min_val=0, max_val=NB * MAXC)
                sums = acc[:, ds(b % 2), 0:WZ].rearrange("p a n -> p (a n)")
                pe.wait_ge(flushed, b + 1)
                pe.wait_ge(qlo_done, b + 2)
                nc.tensor.matmul(sums, zero[:, 0:P], zero[:, :], start=True, stop=False, skip_group_check=True)
                with pe.Fori(0, count) as j:
                    g = pe.snap(before + j)
                    qs = pe.snap((b + (j + 1) // count) % 3)
                    for h in range(2):
                        turn_onehot(g + 1, h)
                        spread(g + 1, h, qs)
                        add_up(g, h, sums)
                nc.tensor.matmul(sums, zero[:, 0:P], zero[:, :], start=False, stop=True,
                                 skip_group_check=True).then_inc(acc_done, 1)

            pe.wait_ge(f_in, 16 * 9)
            pe.wait_ge(flushed, NB + 2)

            def turn_group(G):
                pe.wait_ge(f_prep, (G + 1) * PREP)
                for k in range(4):
                    if k >= 2:
                        pe.wait_ge(f_ft, 4 * G + k - 1)
                    for m in range(4 * k, min(4 * k + 4, 2 * GB)):
                        ins = nc.tensor.transpose(acc[:, k % 2, (m % 4) * P:(m % 4 + 1) * P],
                                                  xn3[:, m // 2, (m % 2) * P:(m % 2 + 1) * P], ident[:, :])
                    ins.then_inc(f_turned, 1)

            def router(G):
                pe.wait_ge(f_ft, 4 * G + 4)
                for hh in range(2):
                    for c in range(2):
                        ins = nc.tensor.matmul(bank[hh][:, 0:HT], rw1_sb[:, c, :],
                                               ft[:, ds(G % 2), c, hh * HT:(hh + 1) * HT].rearrange("p a n -> p (a n)"),
                                               start=c == 0, stop=c == 1)
                    ins.then_inc(f_col, 1)
                pe.wait_ge(f_relu, G * USES + 2)
                for t in range(GB):
                    ins = nc.tensor.matmul(acc[:, 0, t * NE:(t + 1) * NE], rh[:, t * P:(t + 1) * P], rw2_sb[:, :],
                                           start=True, stop=True)
                ins.then_inc(f_logits, 1)

            def turn_gates(G):
                pe.wait_ge(f_gate, (G + 1) * GATES)
                for k in range(2):
                    for t in range(4 * k, min(4 * k + 4, GB)):
                        ins = nc.tensor.transpose(acc[0:NE, k, (t % 4) * P:(t % 4 + 1) * P], gate[:, t, :], ident[:, :])
                    ins.then_inc(f_gturned, 1)

            def hidden(G, e):
                for k in range(8):
                    layer, hh, m = k // 4, k % 4 // 2, k % 2
                    use = 2 + 8 * e + k
                    bank_read = use - 3
                    inputs = 2 + 8 * e + 2 * (hh + 1) if layer else 0
                    if use >= 4:
                        pe.wait_ge(f_relu, G * USES + max(bank_read, inputs))
                    for c in range(2):
                        rhs = (h1[:, c, hh * HT:(hh + 1) * HT] if layer
                               else ft[:, ds(G % 2), c, hh * HT:(hh + 1) * HT].rearrange("p a n -> p (a n)"))
                        ins = nc.tensor.matmul(bank[use % 4][:, 0:HT], (w1_sb, w2_sb)[layer][:, e, c, m * P:(m + 1) * P],
                                               rhs, start=c == 0, stop=c == 1)
                    ins.then_inc(f_col, 1)

            def last(G, e):
                for k in range(PAIRS):
                    pe.wait_ge(f_sum, G * SUMS + e * PAIRS + k + 1)
                    if e < NE and k < 2:
                        pe.wait_ge(f_relu, G * USES + 2 + 8 * e + (6, 8)[k])
                    if e == NE and k == 0:
                        pe.wait_ge(f_gt, 2 * G + 2)
                    for t in range(2 * k, min(2 * k + 2, GB)):
                        o = bank[4 + k % 2][:, (t % 2) * D:(t % 2 + 1) * D]
                        if e == NE:
                            ins = nc.tensor.matmul(o, gt[0:NE, t * P:(t + 1) * P], eb3_sb[:, :], start=True, stop=True)
                        else:
                            for c in range(2):
                                ins = nc.tensor.matmul(o, h2[:, c, t * P:(t + 1) * P], w3_sb[:, e, c, :],
                                                       start=c == 0, stop=c == 1)
                    ins.then_inc(f_last, 1)

            def group(G, more):
                router(G)
                for e in range(NE):
                    hidden(G, e)
                    last(G, e)
                    if e == 2:
                        turn_gates(G)
                        if more:
                            pe.wait_ge(f_gt, 2 * G + 2)
                            turn_group(G + 1)
                last(G, NE)

            turn_group(0)
            with pe.Fori(0, NG - 1) as G:
                group(G, True)
            group(NG - 1, False)

        @block.scalar
        def _(act):
            def root(c):
                act.wait_ge(ve_ready, c + 1)
                nc.scalar.activation(sd[:, c * TPX:(c + 1) * TPX], ve[:, c * TPX:(c + 1) * TPX], ACT.Sqrt).then_inc(sd_ready, 1)

            for u in range(2):
                act.sem_inc(kvs_done[u], 1)
            for h in range(2):
                act.sem_inc(oht_done[h], 1)
            act.sem_inc(flushed, 2)
            for c in range(XC):
                root(c)

            def keep_kv(i):
                for u in range(2):
                    act.wait_ge(kvp_done[u], i + 1)
                    if not isinstance(i, int):
                        act.wait_ge(kv_out[u], 16 * i)
                    nc.scalar.copy(kvs[:, u, :], bank[2 + u][:, :]).then_inc(kvs_done[u], 1)
            keep_kv(0)
            with act.Fori(1, NT // 2) as i:
                keep_kv(i)

            def high(source, slot):
                nc.scalar.copy(qhl[:, ds(slot), 0, :].rearrange("p a d -> p (a d)"),
                               q_sb[:, ds(source), :].rearrange("p a d -> p (a d)")).then_inc(qhi_done, 1)

            def keep_turned(g, h):
                act.wait_ge(ot_done[h], g + 1)
                if not isinstance(g, int):
                    act.wait_ge(spread_done[h], g)
                nc.scalar.copy(oh_t[:, h, :, :].rearrange("p t n -> p (t n)"),
                               bank[h][:, :].bitcast(BF16)[:, 0:TPH * P]).then_inc(oht_done[h], 1)

            def keep_onehot(g, h):
                act.wait_ge(oh_done[h], g + 3)
                act.wait_ge(sum_done[h], g + 1)
                nc.scalar.copy(oh_sum[:, h, :, :], oh[:, h, :, :]).then_inc(keep_done[h], 1)

            def weights(g, h):
                act.wait_ge(clip_done[h], g + 1)
                nc.scalar.activation(wv[:, h, :, D:], clipped[:, h, :, :], ACT.Exp, scale=DK ** -0.5).then_inc(weight_done[h], 1)

            for u in range(2):
                act.wait_ge(q_kept[u], NT // 2 + 1)
            high(0, 0)
            high(1, 1)
            act.wait_ge(table_ready, 1)
            for h in range(2):
                keep_turned(0, h)
            with act.Fori(0, NB) as b:
                count = act.value_load(table[0:1, COUNT, ds(b)], min_val=1, max_val=MAXC)
                before = act.value_load(table[0:1, BEFORE, ds(b)], min_val=0, max_val=NB * MAXC)
                act.wait_ge(prod_done[0], before + 1)
                act.wait_ge(prod_done[1], before + 1)
                high(inside(act.snap((b + 2) - (b + 2) // NT), NT - 1), (b + 2) % 3)
                with act.Fori(0, count) as j:
                    g = act.snap(before + j)
                    for h in range(2):
                        keep_onehot(g, h)
                        weights(g, h)
                        keep_turned(g + 1, h)
                act.wait_ge(acc_done, b + 1)
                nc.scalar.copy(q_sb[:, ds(b), :], acc[:, ds(b % 2), 0:D])
                nc.scalar.copy(z_sb[:, ds(b), :], acc[:, ds(b % 2), D:WZ]).then_inc(flushed, 1)

            act.wait_ge(f_in, 16 * 9)
            act.wait_ge(edges_done, 2)

            def root_group(G):
                act.wait_ge(f_prep, G * PREP + PREP - 2)
                nc.scalar.activation(sd[:, ds(G * GB, GB)], ve[:, ds(G * GB, GB)], ACT.Sqrt).then_inc(f_sqrt, 1)

            def keep_group(G):
                for k in range(4):
                    act.wait_ge(f_turned, 4 * G + k + 1)
                    n = min(4, 2 * GB - 4 * k) // 2
                    nc.scalar.copy(ft[:, ds(G % 2), :, 2 * k * P:(2 * k + n) * P].rearrange("p a c (t n) -> p (a t) c n", n=P),
                                   acc[:, k % 2, 0:2 * n * P].rearrange("p (t c n) -> p t c n", c=2, n=P)).then_inc(f_ft, 1)

            def relu(G, e, ks):
                for k in ks:
                    layer, hh, m = k // 4, k % 4 // 2, k % 2
                    use = 2 + 8 * e + k
                    act.wait_ge(f_col, G * USES + use + 1)
                    col = (layer * NE + e) * 2 + m
                    nc.scalar.activation((h1, h2)[layer][:, m, hh * HT:(hh + 1) * HT], bank[use % 4][:, 0:HT], ACT.Relu,
                                         bias=cols_sb[:, col:col + 1]).then_inc(f_relu, 1)

            def group(G, more):
                for hh in range(2):
                    act.wait_ge(f_col, G * USES + hh + 1)
                    nc.scalar.activation(rh[:, hh * HT:(hh + 1) * HT], bank[hh][:, 0:HT], ACT.Relu,
                                         bias=cols_sb[:, 4 * NE:4 * NE + 1]).then_inc(f_relu, 1)
                act.wait_ge(f_gate, G * GATES + EX_AT)
                nc.scalar.activation(ex[:, :, :], lg[:, :, :], ACT.Exp).then_inc(f_exp, 1)
                for e in range(NE):
                    relu(G, e, range(4))
                    if e == 0:
                        act.wait_ge(f_gate, G * GATES + EE_AT)
                        nc.scalar.activation(ee, dd, ACT.Exp).then_inc(f_exp, 1)
                    if e == 2 and more:
                        root_group(G + 1)
                    relu(G, e, range(4, 8))
                    if e == 2:
                        for k in range(2):
                            act.wait_ge(f_gturned, 2 * G + k + 1)
                            n = min(4, GB - 4 * k) * P
                            nc.scalar.copy(gt[0:NE, 4 * k * P:4 * k * P + n], acc[0:NE, k, 0:n]).then_inc(f_gt, 1)
                        if more:
                            keep_group(G + 1)

            root_group(0)
            keep_group(0)
            with act.Fori(0, NG - 1) as G:
                group(G, True)
            group(NG - 1, False)

        @block.vector
        def _(dve):
            for u in range(2):
                dve.sem_inc(xt_done[u], 1)
                dve.sem_inc(q_kept[u], 1)
            for h in range(2):
                dve.sem_inc(oh_done[h], 2)
                dve.sem_inc(prod_done[h], 1)
                dve.sem_inc(wv_done[h], 2)
            dve.sem_inc(f_sum, 2)
            nc.vector.memset(zero[:, :], 0.0).then_inc(zero_done, 1)
            dve.wait_ge(c_in, 16)
            nc.vector.tensor_copy(identb[:, :], ident[:, :]).then_inc(zero_done, 1)

            stats_next = counter()

            def statistics(c):
                dve.wait_ge(x_in[c], 16)
                for T in range(c * TPX, (c + 1) * TPX):
                    nc.vector.bn_stats(bn[:, T, :], x_sb[:, T, :]).then_inc(stats, 1)
                dve.wait_ge(stats, stats_next(TPX))
                for T in range(c * TPX, (c + 1) * TPX):
                    nc.vector.bn_aggr(mv[:, T, :], bn[:, T, :]).then_inc(stats, 1)
                dve.wait_ge(stats, stats_next(TPX))
                a, z = c * TPX, (c + 1) * TPX
                nc.vector.tensor_scalar(ve[:, a:z], mv[:, a:z, 1:2].rearrange("p a b -> p (a b)"), EPS, None,
                                        ALU.add).then_inc(ve_ready, 1)

            def inverse(c):
                a, z = c * TPX, (c + 1) * TPX
                dve.wait_ge(sd_ready, c + 1)
                nc.vector.reciprocal(rstd[:, a:z], sd[:, a:z]).then_inc(rstd_ready, 1)

            bounds_next = counter()

            def find_ends():
                dve.wait_ge(e_in, 16)
                dve.wait_ge(iota_done, 4)
                dst = edges_sb[:, :, :, 1:2].rearrange("p u e c -> p u (e c)")
                nc.vector.tensor_reduce(umin, dst, AX, ALU.min).then_inc(bounds, 1)
                dve.wait_ge(bounds, bounds_next())
                nc.vector.tensor_reduce(umax, dst, AX, ALU.max).then_inc(bounds, 1)
                dve.wait_ge(bounds, bounds_next())
                nc.vector.tensor_copy(lo_f, iota_i[:, 0:NB]).then_inc(bounds, 1)
                dve.wait_ge(bounds, bounds_next())
                nc.vector.tensor_copy(hi_f, iota_i[:, NB:2 * NB]).then_inc(bounds, 1)
                dve.wait_ge(bounds, bounds_next())
                nc.vector.tensor_copy(unit_f, iota_i[:, 2 * NB:]).then_inc(bounds, 1)
                dve.wait_ge(bounds, bounds_next())

                left, upto = tf[:, 0, :], tf[:, 1, :]
                nc.vector.tensor_scalar(left, unit_f, -1.0, float(UPAD), ALU.mult, ALU.add).then_inc(bounds, 1)
                dve.wait_ge(bounds, bounds_next())
                nc.vector.tensor_scalar(upto, unit_f, 1.0, None, ALU.add).then_inc(bounds, 1)
                dve.wait_ge(bounds, bounds_next())
                for b0 in range(0, NB, HB):
                    n = min(HB, NB - b0)

                    def by_unit(v):
                        return v.rearrange("p (a u) -> p a u", a=1).to_broadcast([P, n, UPP])

                    def by_block(v):
                        return v[:, b0:b0 + n].rearrange("p (b a) -> p b a", a=1).to_broadcast([P, n, UPP])
                    one, two = inter[:, 0:n, :], inter2[:, 0:n, :]
                    nc.vector.tensor_tensor(one, by_unit(umin), by_block(hi_f), ALU.is_le).then_inc(bounds, 1)
                    dve.wait_ge(bounds, bounds_next())
                    nc.vector.tensor_tensor(two, by_unit(umax), by_block(lo_f), ALU.is_ge).then_inc(bounds, 1)
                    dve.wait_ge(bounds, bounds_next())
                    nc.vector.tensor_tensor(one, one, two, ALU.mult).then_inc(bounds, 1)
                    dve.wait_ge(bounds, bounds_next())
                    for k, v in enumerate((left, upto)):
                        nc.vector.tensor_tensor(two, one, by_unit(v), ALU.mult).then_inc(bounds, 1)
                        dve.wait_ge(bounds, bounds_next())
                        nc.vector.tensor_reduce(ends[:, k, b0:b0 + n], two, AX, ALU.max).then_inc(bounds, 1)
                        dve.wait_ge(bounds, bounds_next())
                dve.sem_inc(ends_ready, 1)

            def write_table():
                dve.wait_ge(ends_reduced, 1)
                some, first, length, count, ones, upto = (tf[:, k, :] for k in range(6))
                ci = table[:, COUNT, :]
                nc.vector.tensor_scalar(some, ends_all[:, 0, :], 0.0, None, ALU.is_gt).then_inc(bounds, 1)
                dve.wait_ge(bounds, bounds_next())
                nc.vector.tensor_scalar(first, ends_all[:, 0, :], -1.0, float(UPAD), ALU.mult, ALU.add).then_inc(bounds, 1)
                dve.wait_ge(bounds, bounds_next())
                nc.vector.tensor_tensor(first, first, some, ALU.mult).then_inc(bounds, 1)
                dve.wait_ge(bounds, bounds_next())
                nc.vector.tensor_copy(table[:, FIRST, :], first).then_inc(bounds, 1)
                dve.wait_ge(bounds, bounds_next())
                nc.vector.tensor_tensor(length, ends_all[:, 1, :], first, ALU.subtract).then_inc(bounds, 1)
                dve.wait_ge(bounds, bounds_next())
                nc.vector.tensor_scalar(ci, length, float(UPS - 1), None, ALU.add).then_inc(bounds, 1)
                dve.wait_ge(bounds, bounds_next())
                nc.vector.tensor_scalar(ci, ci, UPS.bit_length() - 1, None, ALU.arith_shift_right).then_inc(bounds, 1)
                dve.wait_ge(bounds, bounds_next())
                nc.vector.tensor_scalar(ci, ci, 1.0, None, ALU.max).then_inc(bounds, 1)
                dve.wait_ge(bounds, bounds_next())
                nc.vector.tensor_copy(count, ci).then_inc(bounds, 1)
                dve.wait_ge(bounds, bounds_next())
                nc.vector.memset(ones, 1.0).then_inc(bounds, 1)
                dve.wait_ge(bounds, bounds_next())
                nc.vector.tensor_tensor_scan(upto, ones, count, 0.0, ALU.mult, ALU.add).then_inc(bounds, 1)
                dve.wait_ge(bounds, bounds_next())
                nc.vector.tensor_tensor(table[:, BEFORE, :], upto, count, ALU.subtract).then_inc(bounds, 1)
                dve.wait_ge(bounds, bounds_next())
                nc.vector.tensor_copy(pairs[:, :], upto[:, NB - 1:NB]).then_inc(bounds, 1)
                dve.wait_ge(bounds, bounds_next())
                nc.vector.tensor_scalar(odd[:, :], pairs[:, :], 1, None, ALU.bitwise_and).then_inc(bounds, 1)
                dve.wait_ge(bounds, bounds_next())
                nc.vector.tensor_tensor(pairs[:, :], pairs[:, :], odd[:, :], ALU.add).then_inc(bounds, 1)
                dve.wait_ge(bounds, bounds_next())
                nc.vector.tensor_scalar(pairs[:, :], pairs[:, :], 1, None, ALU.arith_shift_right).then_inc(bounds, 1)
                dve.wait_ge(bounds, bounds_next())
                nc.vector.tensor_tensor(ci[:, NB - 1:NB], ci[:, NB - 1:NB], odd[:, :], ALU.add).then_inc(bounds, 1)
                dve.wait_ge(bounds, bounds_next())
                nc.vector.tensor_copy(table[:, LOADS, :], ci).then_inc(bounds, 1)
                dve.wait_ge(bounds, bounds_next())
                nc.vector.tensor_scalar(table[:, LOADS, NB - 1:NB], ci[:, NB - 1:NB], 1.0, None, ALU.add).then_inc(table_ready, 1)

            def normalise(i, u):
                dve.wait_ge(tp_done[u], i + 1)
                T = 2 * i + u
                nc.vector.tensor_scalar(xn[:, u, :], x_sb[:, ds(T), :].rearrange("p a b -> p (a b)"),
                                        mv[:, ds(T), 0:1].rearrange("p a b -> p (a b)"), rstd[:, ds(T)],
                                        ALU.subtract, ALU.mult).then_inc(xn_done[u], 1)

            def keep_x(i, u):
                dve.wait_ge(tp_done[u], i + 2)
                nc.vector.tensor_copy(xt[:, u, :, :].rearrange("p c n -> p (c n)"), bank[u][:, 0:D]).then_inc(xt_done[u], 1)

            def keep_q(i, u):
                dve.wait_ge(qp_done[u], i + 1)
                nc.vector.tensor_copy(q_sb[:, ds(2 * i + u), :].rearrange("p a d -> p (a d)"), bank[4 + u][:, 0:D]).then_inc(q_kept[u], 1)

            for c in range(XC):
                statistics(c)
                inverse(c)
                if c == 0:
                    find_ends()
            dve.wait_ge(rstd_ready, XC)
            normalise(0, 0)
            normalise(0, 1)
            keep_x(0, 0)
            with dve.Fori(0, NT // 2 - 1) as i:
                keep_x(i, 1)
                normalise(i + 1, 0)
                keep_q(i, 0)
                keep_x(i + 1, 0)
                normalise(i + 1, 1)
                keep_q(i, 1)
            keep_x(NT // 2 - 1, 1)
            keep_q(NT // 2 - 1, 0)
            keep_q(NT // 2 - 1, 1)
            write_table()

            def low(b):
                dve.wait_ge(qhi_done, b + 1)
                part_ = qhl[:, ds(b % 3), :, :]
                nc.vector.tensor_tensor(part_[:, :, 1, :], q_sb[:, ds(b), :], part_[:, :, 0, :].bitcast(F32),
                                        ALU.subtract).then_inc(qlo_done, 1)

            def onehots(g, h, slot, block_):
                dve.wait_ge(idx_seen, 2 * g + h + 1)
                if not isinstance(g, int):
                    dve.wait_ge(keep_done[h], g)
                    dve.wait_ge(ot_done[h], g)
                for t in range(TPH):
                    ins = nc.vector.tensor_scalar(oh[:, h, t, :], nodes[:, ds(block_ * P, P)],
                                                  idx[:, ds(slot), t, 1:2].rearrange("p a c -> p (a c)"), None, ALU.is_equal)
                ins.then_inc(oh_done[h], 1)

            def rows(slot, a, z):
                return ring[:, ds(slot), :, a:z].rearrange("p a t d -> p (a t) d")

            def multiply(g, h, slot):
                dve.wait_ge(kv_seen, 2 * g + (h + 5))
                dve.wait_ge(spread_done[h], g + 1)
                nc.vector.tensor_tensor(prod[:, :, :], rows(slot, 0, D), bank[2 + h][:, :].rearrange("p (t d) -> p t d", t=TPH),
                                        ALU.mult).then_inc(prod_done[h], 1)

            def score_of(g, h):
                dve.wait_ge(prod_done[h], g + 2)
                nc.vector.tensor_reduce(score[:, h, :, :].rearrange("p t h -> p (t h)"),
                                        prod[:, :, :].rearrange("p t (h k) -> p (t h) k", k=DK), AX, ALU.add).then_inc(score_done[h], 1)
                dve.wait_ge(score_done[h], g + 1)
                nc.vector.tensor_scalar(clipped[:, h, :, :], score[:, h, :, :], CLIP, -CLIP, ALU.min, ALU.max).then_inc(clip_done[h], 1)

            def weigh(g, h, slot):
                dve.wait_ge(weight_done[h], g + 1)
                nc.vector.tensor_tensor(
                    wv[:, h, :, 0:D].rearrange("p t (h k) -> p t h k", k=DK),
                    rows(slot, D, KV).rearrange("p t (h k) -> p t h k", k=DK),
                    wv[:, h, :, D:].rearrange("p t (h a) -> p t h a", a=1).to_broadcast([P, TPH, H, DK]),
                    ALU.mult).then_inc(wv_done[h], 1)

            low(0)
            for h in range(2):
                onehots(0, h, h, 0)
            with dve.Fori(0, NB) as b:
                count = dve.value_load(table[0:1, COUNT, ds(b)], min_val=1, max_val=MAXC)
                before = dve.value_load(table[0:1, BEFORE, ds(b)], min_val=0, max_val=NB * MAXC)
                low(b + 1)
                with dve.Fori(0, count) as j:
                    g = dve.snap(before + j)
                    slot = dve.snap((g % 2) * 2)
                    early = inside(dve.snap(b + (j + 1) // count), NB)
                    multiply(g, 0, slot)
                    score_of(g, 0)
                    onehots(g + 1, 0, (slot + 2) % 4, early)
                    multiply(g, 1, slot + 1)
                    weigh(g, 0, slot)
                    score_of(g, 1)
                    onehots(g + 1, 1, (slot + 2) % 4 + 1, early)
                    weigh(g, 1, slot + 1)

            dve.drain().then_inc(edges_done, 1)
            dve.wait_ge(f_in, 16 * 9)
            dve.wait_ge(edges_done, 2)
            dve.wait_ge(flushed, NB + 2)

            def prepare(G):
                step = counter()
                blocks = ds(G * GB, GB)
                nc.vector.tensor_scalar(ze, z_sb[:, blocks, :], 1e-9, None, ALU.add).then_inc(f_prep, 1)
                dve.wait_ge(f_prep, G * PREP + step())
                nc.vector.reciprocal(zr, ze).then_inc(f_prep, 1)
                dve.wait_ge(f_prep, G * PREP + step())
                u = q_sb[:, blocks, :].rearrange("p t (h k) -> p t h k", k=DK)
                nc.vector.tensor_tensor(u, u, zr.rearrange("p t (h a) -> p t h a", a=1).to_broadcast([P, GB, H, DK]), ALU.mult).then_inc(f_prep, 1)
                dve.wait_ge(f_prep, G * PREP + step())
                nc.vector.tensor_tensor(x_sb[:, blocks, :], x_sb[:, blocks, :], q_sb[:, blocks, :], ALU.add).then_inc(f_prep, 1)
                dve.wait_ge(f_prep, G * PREP + step())
                dve.sem_inc(f_mark, 1)
                for t in range(GB):
                    nc.vector.bn_stats(bn[:, t, :], x_sb[:, ds(G * GB + t), :].rearrange("p a d -> p (a d)")).then_inc(f_prep, 1)
                dve.wait_ge(f_prep, G * PREP + step(GB))
                dve.sem_inc(f_mark, 1)
                for t in range(GB):
                    nc.vector.bn_aggr(mv[:, t, :], bn[:, t, :]).then_inc(f_prep, 1)
                dve.wait_ge(f_prep, G * PREP + step(GB))
                nc.vector.tensor_scalar(ve[:, blocks], mv[:, 0:GB, 1:2].rearrange("p a b -> p (a b)"), EPS, None, ALU.add).then_inc(f_prep, 1)
                dve.wait_ge(f_sqrt, G + 1)
                nc.vector.reciprocal(rstd[:, blocks], sd[:, blocks]).then_inc(f_prep, 1)
                dve.wait_ge(f_prep, G * PREP + step(2))
                if not isinstance(G, int):
                    dve.wait_ge(f_turned, 4 * G)
                for t in range(GB):
                    ins = nc.vector.tensor_scalar(xn3[:, t, :], x_sb[:, ds(G * GB + t), :].rearrange("p a d -> p (a d)"),
                                                  mv[:, t, 0:1], rstd[:, ds(G * GB + t)], ALU.subtract, ALU.mult)
                ins.then_inc(f_prep, 1)
                assert step() == PREP

            def route(G):
                step = counter()

                def each(v):
                    return v.rearrange("p (t a) -> p t a", a=1).to_broadcast([P, GB, NE])
                dve.wait_ge(f_logits, G + 1)
                nc.vector.tensor_tensor(lg, acc[:, 0, 0:GB * NE].rearrange("p (t e) -> p t e", e=NE),
                                        rb2_sb[:, :].rearrange("p (a e) -> p a e", a=1).to_broadcast([P, GB, NE]), ALU.add).then_inc(f_gate, 1)
                dve.wait_ge(f_gate, G * GATES + step())
                nc.vector.tensor_reduce(m0, lg, AX, ALU.max).then_inc(f_gate, 1)
                dve.wait_ge(f_gate, G * GATES + step())
                nc.vector.tensor_tensor(lg, lg, each(m0), ALU.subtract).then_inc(f_gate, 1)
                dve.wait_ge(f_gate, G * GATES + step())
                assert step(0) == EX_AT
                dve.wait_ge(f_exp, 2 * G + 1)
                nc.vector.tensor_reduce(se, ex, AX, ALU.add).then_inc(f_gate, 1)
                dve.wait_ge(f_gate, G * GATES + step())
                nc.vector.reciprocal(rse, se).then_inc(f_gate, 1)
                dve.wait_ge(f_gate, G * GATES + step())
                nc.vector.tensor_tensor(pr, ex, each(rse), ALU.mult).then_inc(f_gate, 1)
                dve.wait_ge(f_gate, G * GATES + step())
                of_e = pr.rearrange("p t (e a) -> p t e a", a=1).to_broadcast([P, GB, NE, NE])
                of_j = pr.rearrange("p t (a j) -> p t a j", a=1).to_broadcast([P, GB, NE, NE])
                low_ = lower[:, :, :].rearrange("p (a e) j -> p a e j", a=1).to_broadcast([P, GB, NE, NE])
                nc.vector.tensor_tensor(above, of_j, of_e, ALU.is_gt).then_inc(f_gate, 1)
                dve.wait_ge(f_gate, G * GATES + step())
                nc.vector.tensor_tensor(equal, of_j, of_e, ALU.is_equal).then_inc(f_gate, 1)
                dve.wait_ge(f_gate, G * GATES + step())
                nc.vector.tensor_tensor(equal, equal, low_, ALU.mult).then_inc(f_gate, 1)
                dve.wait_ge(f_gate, G * GATES + step())
                nc.vector.tensor_tensor(above, above, equal, ALU.add).then_inc(f_gate, 1)
                dve.wait_ge(f_gate, G * GATES + step())
                nc.vector.tensor_reduce(rank, above, AX, ALU.add).then_inc(f_gate, 1)
                dve.wait_ge(f_gate, G * GATES + step())
                nc.vector.tensor_scalar(sel1, rank, 0.0, None, ALU.is_equal).then_inc(f_gate, 1)
                dve.wait_ge(f_gate, G * GATES + step())
                nc.vector.tensor_scalar(sel2, rank, 1.0, None, ALU.is_equal).then_inc(f_gate, 1)
                dve.wait_ge(f_gate, G * GATES + step())
                nc.vector.tensor_reduce(t1, pr, AX, ALU.max).then_inc(f_gate, 1)
                dve.wait_ge(f_gate, G * GATES + step())
                nc.vector.tensor_tensor(tmp, pr, sel2, ALU.mult).then_inc(f_gate, 1)
                dve.wait_ge(f_gate, G * GATES + step())
                nc.vector.tensor_reduce(t2, tmp, AX, ALU.add).then_inc(f_gate, 1)
                dve.wait_ge(f_gate, G * GATES + step())
                nc.vector.tensor_tensor(dd, t2, t1, ALU.subtract).then_inc(f_gate, 1)
                dve.wait_ge(f_gate, G * GATES + step())
                assert step(0) == EE_AT
                dve.wait_ge(f_exp, 2 * G + 2)
                nc.vector.tensor_scalar(e1, ee, 1.0, None, ALU.add).then_inc(f_gate, 1)
                dve.wait_ge(f_gate, G * GATES + step())
                nc.vector.reciprocal(wt1, e1).then_inc(f_gate, 1)
                dve.wait_ge(f_gate, G * GATES + step())
                nc.vector.tensor_tensor(wt2, wt1, ee, ALU.mult).then_inc(f_gate, 1)
                dve.wait_ge(f_gate, G * GATES + step())
                nc.vector.tensor_tensor(sel1, sel1, each(wt1), ALU.mult).then_inc(f_gate, 1)
                dve.wait_ge(f_gate, G * GATES + step())
                nc.vector.tensor_tensor(sel2, sel2, each(wt2), ALU.mult).then_inc(f_gate, 1)
                dve.wait_ge(f_gate, G * GATES + step())
                nc.vector.tensor_tensor(gate, sel1, sel2, ALU.add).then_inc(f_gate, 1)
                dve.wait_ge(f_gate, G * GATES + step())
                assert step(0) == GATES

            def combine(G, e):
                for k in range(PAIRS):
                    use = G * SUMS + (e * PAIRS + k)
                    dve.wait_ge(f_last, use + 1)
                    if e:
                        dve.wait_ge(f_sum, use - 1)
                    for t in range(2 * k, min(2 * k + 2, GB)):
                        o = bank[4 + k % 2][:, (t % 2) * D:(t % 2 + 1) * D]
                        xt_ = x_sb[:, ds(G * GB + t), :].rearrange("p a d -> p (a d)")
                        if e == NE:
                            ins = nc.vector.tensor_tensor(xt_, o, xt_, ALU.add)
                        else:
                            ins = nc.vector.scalar_tensor_tensor(xt_, o, gate[:, t, e:e + 1], xt_, ALU.mult, ALU.add)
                    ins.then_inc(f_sum, 1)

            def group(G, more):
                route(G)
                for e in range(NE + 1):
                    combine(G, e)
                    if e == 1 and more:
                        prepare(G + 1)

            prepare(0)
            with dve.Fori(0, NG - 1) as G:
                group(G, True)
            group(NG - 1, False)


def kernel(x, src, dst, L0_gnn_Wq, L0_gnn_Wk, L0_gnn_Wv, L0_ffn_router_w1, L0_ffn_router_b1, L0_ffn_router_w2,
           L0_ffn_router_b2, L0_ffn_expert_w1, L0_ffn_expert_b1, L0_ffn_expert_w2, L0_ffn_expert_b2,
           L0_ffn_expert_w3, L0_ffn_expert_b3):
    import numpy as np
    import concourse.bacc as bacc
    from concourse.bass_utils import run_bass_kernel_spmd

    def f(a):
        return np.ascontiguousarray(np.asarray(a))

    xp = np.zeros((NT * P, D), np.float32)
    xp[:N] = f(x)
    edges = np.zeros((EPAD, 2), np.int32)
    edges[:, 1] = FAR
    edges[:E, 0] = f(src)
    edges[:E, 1] = f(dst)

    def columns(b):
        return f(b).reshape(-1, P).T

    arrays = {
        "x": xp,
        "edges": edges,
        "wkvq": np.concatenate([f(L0_gnn_Wk), f(L0_gnn_Wv), f(L0_gnn_Wq)], axis=1),
        "rw1": f(L0_ffn_router_w1),
        "rw2": f(L0_ffn_router_w2),
        "rb2": f(L0_ffn_router_b2),
        "w1": f(L0_ffn_expert_w1),
        "w2": f(L0_ffn_expert_w2),
        "w3": f(L0_ffn_expert_w3),
        "eb3": f(L0_ffn_expert_b3),
        "cols": np.ascontiguousarray(np.concatenate(
            [columns(L0_ffn_expert_b1), columns(L0_ffn_expert_b2), columns(L0_ffn_router_b1)], axis=1)),
        "ident": np.eye(P, dtype=np.float32),
        "lower": np.tril(np.ones((NE, NE), np.float32), -1).reshape(1, NE * NE),
    }
    nc = bacc.Bacc("TRN2", target_bir_lowering=False, num_devices=1)
    args = [nc.dram_tensor("in_" + name, a.shape, mybir.dt.from_np(a.dtype), kind="ExternalInput").ap() for name, a in arrays.items()]
    kv_table = nc.dram_tensor("kv_table", (NT * P, KV), F32, kind="Internal").ap()
    out = nc.dram_tensor("out", (NB * P, D), F32, kind="ExternalOutput").ap()
    gnn_ffn(nc, *args, kv_table, out)
    r = run_bass_kernel_spmd(nc, [{"in_" + name: a for name, a in arrays.items()}], core_ids=[0])
    return r.results[0]["out"][:N]
```
